# Optimizing a Trainium2 kernel written in Bass

```python
import numpy as np
import jax
import jax.numpy as jnp

def _softmax(x, axis=-1):
    return jax.nn.softmax(x, axis=axis)
def _gelu(x):
    return jax.nn.gelu(x, approximate=True)
def _silu(x):
    return jax.nn.silu(x)
def _sigmoid(x):
    return jax.nn.sigmoid(x)
def _layernorm(x, axis=-1, eps=1e-5):
    m = jnp.mean(x, axis=axis, keepdims=True)
    v = jnp.var(x, axis=axis, keepdims=True)
    return (x - m) / jnp.sqrt(v + eps)
def _scatter_add(tgt, idx, src, axis=0):
    return tgt.at[idx].add(src)
def _segment_sum(src, seg, n):
    return jax.ops.segment_sum(src, seg, n)

kernel_name = 'mk_conv_seq_d1_conv_nchw512_bafcd7'

def setup_inputs(seed: int = 0):
    np.random.seed(seed)
    _w = jnp.asarray
    def _rec_inputs():
        import jax
        import jax.numpy as jnp
        _gk = jax.random.key(seed)
        x = -0.000125 + 0.9999 * jax.random.normal(jax.random.fold_in(_gk, 1), (16, 512, 64, 64), jnp.float32)
        return x
    x = _rec_inputs()
    def _L0_conv_setup():
        import jax, jax.numpy as jnp
        import numpy as np
        from jax import lax
        IN_DIM = 512
        MID = IN_DIM // 2
        HEADS = 8
        B, H, W = (16, 64, 64)
        BN_EPS = 1e-05
        NORM_EPS = 1e-12
        key = jax.random.key(seed)
        ks = jax.random.split(key, 16)
        r = lambda k, shape, s=0.02: jax.random.normal(k, shape, dtype=jnp.float32) * s
        return {'x': jax.random.normal(ks[0], (B, IN_DIM, H, W), dtype=jnp.float32), 'reduce_w': r(ks[1], (MID, IN_DIM)), 'reduce_b': jnp.zeros((MID,), jnp.float32), 'dw_w': r(ks[2], (MID, 1, 3, 3), 0.1), 'dw_b': jnp.zeros((MID,), jnp.float32), 'bn_gamma': jnp.ones((MID,), jnp.float32), 'bn_beta': jnp.zeros((MID,), jnp.float32), 'bn_mean': r(ks[3], (MID,), 0.1), 'bn_var': jnp.ones((MID,), jnp.float32), 'gate_w1': r(ks[4], (MID // 8, MID)), 'gate_b1': jnp.zeros((MID // 8,), jnp.float32), 'gate_w2': r(ks[5], (MID, MID // 8)), 'gate_b2': jnp.zeros((MID,), jnp.float32), 'temperature': jnp.ones((HEADS, 1, 1), jnp.float32), 'post_w': r(ks[6], (IN_DIM, 2 * MID)), 'post_b': jnp.zeros((IN_DIM,), jnp.float32)}
    _L0_conv_all = _L0_conv_setup()
    _L0_conv_in = {k: v for k, v in _L0_conv_all.items() if k in ('reduce_w', 'reduce_b', 'dw_w', 'dw_b', 'bn_gamma', 'bn_beta', 'bn_mean', 'bn_var', 'gate_w1', 'gate_b1', 'gate_w2', 'gate_b2', 'temperature', 'post_w', 'post_b', )}
    del _L0_conv_all

    return {
        "x": x,
        "L0_conv_reduce_w": _L0_conv_in["reduce_w"],
        "L0_conv_reduce_b": _L0_conv_in["reduce_b"],
        "L0_conv_dw_w": _L0_conv_in["dw_w"],
        "L0_conv_dw_b": _L0_conv_in["dw_b"],
        "L0_conv_bn_gamma": _L0_conv_in["bn_gamma"],
        "L0_conv_bn_beta": _L0_conv_in["bn_beta"],
        "L0_conv_bn_mean": _L0_conv_in["bn_mean"],
        "L0_conv_bn_var": _L0_conv_in["bn_var"],
        "L0_conv_gate_w1": _L0_conv_in["gate_w1"],
        "L0_conv_gate_b1": _L0_conv_in["gate_b1"],
        "L0_conv_gate_w2": _L0_conv_in["gate_w2"],
        "L0_conv_gate_b2": _L0_conv_in["gate_b2"],
        "L0_conv_temperature": _L0_conv_in["temperature"],
        "L0_conv_post_w": _L0_conv_in["post_w"],
        "L0_conv_post_b": _L0_conv_in["post_b"],
    }

def reference(x, L0_conv_reduce_w, L0_conv_reduce_b, L0_conv_dw_w, L0_conv_dw_b, L0_conv_bn_gamma, L0_conv_bn_beta, L0_conv_bn_mean, L0_conv_bn_var, L0_conv_gate_w1, L0_conv_gate_b1, L0_conv_gate_w2, L0_conv_gate_b2, L0_conv_temperature, L0_conv_post_w, L0_conv_post_b):
    import jax
    import jax.numpy as jnp
    def _L0_conv_ref(x, reduce_w, reduce_b, dw_w, dw_b, bn_gamma, bn_beta, bn_mean, bn_var, gate_w1, gate_b1, gate_w2, gate_b2, temperature, post_w, post_b):
        import jax, jax.numpy as jnp
        import numpy as np
        from jax import lax
        IN_DIM = 512
        MID = IN_DIM // 2
        HEADS = 8
        B, H, W = (16, 64, 64)
        BN_EPS = 1e-05
        NORM_EPS = 1e-12
        Bsz, C, Hh, Ww = x.shape
        xr = jnp.einsum('bchw,oc->bohw', x, reduce_w) + reduce_b[:, None, None]
        xr = lax.conv_general_dilated(xr, dw_w, (1, 1), 'SAME', feature_group_count=MID, dimension_numbers=('NCHW', 'OIHW', 'NCHW'))
        xr = xr + dw_b[:, None, None]
        inv = bn_gamma / jnp.sqrt(bn_var + BN_EPS)
        xr = (xr - bn_mean[:, None, None]) * inv[:, None, None] + bn_beta[:, None, None]
        xr = jax.nn.relu(xr)
        fft_feat = jnp.fft.fft2(xr, norm='ortho')
        HWn = Hh * Ww
        qkv = fft_feat.reshape(Bsz, HEADS, MID // HEADS, HWn)
        nrm = jnp.sqrt(jnp.sum(jnp.abs(qkv) ** 2, axis=-1, keepdims=True))
        qn = qkv / jnp.maximum(nrm, NORM_EPS)
        attn = jnp.einsum('bhcn,bhdn->bhcd', qn, qn)
        attn = attn * temperature
        attn = jax.nn.softmax(attn.real, axis=-1)
        out = jnp.einsum('bhcd,bhdn->bhcn', attn, qkv.real)
        out = out.reshape(Bsz, MID, Hh, Ww).astype(jnp.complex64)
        out = jnp.fft.ifft2(out, norm='ortho').real
        g = jnp.mean(xr, axis=(-2, -1))
        g = jax.nn.relu(g @ gate_w1.T + gate_b1)
        g = jax.nn.sigmoid(g @ gate_w2.T + gate_b2)
        gated = g[:, :, None, None] * xr
        fwm = jnp.fft.ifft2(fft_feat * jnp.fft.fft2(gated)).real
        fused = jnp.concatenate([out, fwm], axis=1)
        y = jnp.einsum('bchw,oc->bohw', fused, post_w) + post_b[:, None, None] + x
        return y

    def _gn(v, G=32, eps=1e-5):
        B_, C_, H_, W_ = v.shape
        g = v.reshape(B_, G, C_ // G, H_, W_)
        m = jnp.mean(g, axis=(2, 3, 4), keepdims=True)
        s = jnp.var(g, axis=(2, 3, 4), keepdims=True)
        return ((g - m) / jnp.sqrt(s + eps)).reshape(v.shape)

    def _ln_c(v, eps=1e-6):
        m = jnp.mean(v, axis=1, keepdims=True)
        s = jnp.var(v, axis=1, keepdims=True)
        return (v - m) / jnp.sqrt(s + eps)

    def _ln_t(v, eps=1e-5):
        m = jnp.mean(v, axis=-1, keepdims=True)
        s = jnp.var(v, axis=-1, keepdims=True)
        return (v - m) / jnp.sqrt(s + eps)

    def _to_tokens(v):
        B_, C_, H_, W_ = v.shape
        return v.reshape(B_, C_, H_ * W_).transpose(0, 2, 1)
    def _from_tokens(t, like):
        B_, C_, H_, W_ = like.shape
        return t.transpose(0, 2, 1).reshape(B_, C_, H_, W_)

    x = _L0_conv_ref(x, L0_conv_reduce_w, L0_conv_reduce_b, L0_conv_dw_w, L0_conv_dw_b, L0_conv_bn_gamma, L0_conv_bn_beta, L0_conv_bn_mean, L0_conv_bn_var, L0_conv_gate_w1, L0_conv_gate_b1, L0_conv_gate_w2, L0_conv_gate_b2, L0_conv_temperature, L0_conv_post_w, L0_conv_post_b)
    return x


_drawn_inputs = setup_inputs


def setup_inputs(seed=0):
    import zlib

    import numpy as np

    out = dict(_drawn_inputs(seed))
    spreads = {'L0_conv_reduce_b': (0.0, 0.1),
     'L0_conv_dw_b': (0.0, 0.1),
     'L0_conv_bn_gamma': (1.0, 0.2),
     'L0_conv_bn_beta': (0.0, 0.1),
     'L0_conv_bn_var': (1.0, 0.2),
     'L0_conv_gate_b1': (0.0, 0.8),
     'L0_conv_gate_b2': (0.0, 0.481),
     'L0_conv_temperature': (1.0, 0.6),
     'L0_conv_post_b': (0.0, 0.1)}
    factors = {'L0_conv_reduce_w': 6.675, 'L0_conv_gate_w1': 8.0, 'L0_conv_gate_w2': 8.0}
    for name, (base, spread) in spreads.items():
        noise = np.random.default_rng([zlib.crc32(name.encode()), seed]).standard_normal(out[name].shape)
        drawn = base * np.exp(spread * noise) if base else spread * noise
        out[name] = jnp.asarray(drawn.astype(out[name].dtype))
    for name, factor in factors.items():
        out[name] = (out[name] * factor).astype(out[name].dtype)
    return out
```

```python
from contextlib import ExitStack

import numpy as np

import concourse.bass as bass
from concourse import mybir


F32 = mybir.dt.float32
ALU = mybir.AluOpType
ACT = mybir.ActivationFunctionType
AX_X = mybir.AxisListType.X

P = 128
S = 64
CH = 512
NCH = S * S // CH
BN_EPS = 1e-5
NORM_EPS = 1e-12
TAPS = [0, 1, 2, 3, 5, 6, 7, 8]
CONV_ROWS = 16
NCONV = S // CONV_ROWS
CONV_OPS = len(TAPS) * 2
CONV_PER_POST = 5
TSLOTS = 4
PSLOTS = 3


def fourier_matrices():
    n = np.arange(S)
    ang = 2 * np.pi * np.outer(n, n) / S
    c, s = np.cos(ang) / 8, np.sin(ang) / 8
    eye2 = np.eye(2)
    alt = (-1.0) ** n / 8
    row = np.stack([c[:, :32], -s[:, :32]], axis=2)
    row[:, 0, 0], row[:, 0, 1] = 1 / 8, alt
    d1 = np.einsum("wkr,ab->awkrb", row, eye2).reshape(P, P)
    d2 = np.block([[c, -s], [s, c]])
    lane = np.zeros((2, S, 2, S))
    for r in range(2):
        lane[r, :, 0, 32 * r:32 * r + 32] = row[:, :, 0]
        lane[r, :, 1, 32 * r:32 * r + 32] = row[:, :, 1]
    lane[0, :, :, 0] = row[:, 0, :]
    d2s = lane.reshape(P, P)
    d3 = np.block([[c, s], [-s, c]])
    back = np.stack([2 * c[:32, :], -2 * s[:32, :]], axis=1)
    back[0, 0, :], back[0, 1, :] = 1 / 8, alt
    unlane = np.zeros((2, S, 2, S))
    for r in range(2):
        unlane[0, 32 * r:32 * r + 32, r, :] = back[:, 0, :]
        unlane[1, 32 * r:32 * r + 32, r, :] = back[:, 1, :]
    d3s = unlane.reshape(P, P)
    d4 = np.einsum("krw,ab->krabw", back, eye2).reshape(P, P)
    return np.stack([d1, d2, d2s, d3, d3s, d4], axis=1).astype(np.float32)


D1, D2, D2S, D3, D3S, D4 = range(6)


def unit_order(with_next):
    order = [("CS", 0), ("T1", 0), ("R1", 0)]
    next_chunk = 0

    def reduce_next():
        nonlocal next_chunk
        if with_next:
            order.append(("A", next_chunk))
        next_chunk += 1

    for i in range(1, 8):
        order.append(("T1", i))
        if i % 4 < 3:
            order.append(("R1", i))
        order.append(("D1", i - 1))
        if i in (3, 6):
            reduce_next()
    order += [("D1", 7)]
    for j in range(8 + 3):
        if j < 8:
            order.append(("T2", j))
        if 1 <= j < 9:
            order.append(("D2", j - 1))
        if 2 <= j < 10:
            order.append(("T3", j - 2))
        if 3 <= j:
            order.append(("D3", j - 3))
        if j in (0, 3, 5, 7):
            reduce_next()
        if j == 8:
            order.append(("W", 0))
    reduce_next()
    order += [("T4", 0)]
    reduce_next()
    order += [("D4", 0)]
    for i in range(8):
        if i + 1 < 8:
            order.append(("T4", i + 1))
        order.append(("P0", i))
        if i + 1 < 8:
            order.append(("D4", i + 1))
        order.append(("P1", i))
    assert next_chunk == NCH
    return order


def build(nc, x, reduce_wt, dw, channel, bias_out, gate_w1t, gate_b1, gate_w2t, post_wt, fourier, identity, out):
    B = x.shape[0]
    KT = x.shape[1] // P
    CT = reduce_wt.shape[2] // P
    HG = gate_w1t.shape[2]

    order, order_last = unit_order(True), unit_order(False)
    PRE = NCH
    PER = len(order)
    assert PER % PSLOTS == 0
    place = {u: n for n, u in enumerate(order)}
    place_last = {u: n for n, u in enumerate(order_last)}
    transposed = {u: n for n, u in enumerate([u for u in order if u[0] in ("T1", "R1", "T2", "T3", "T4")])}
    used_by = {"T1": "D1", "R1": "D1", "T2": "D2", "T3": "D3", "T4": "D4"}
    made = list(transposed)
    for n, u in enumerate(made):
        if n >= TSLOTS:
            v = made[n - TSLOTS]
            for pl in (place, place_last):
                assert pl[(used_by[v[0]], v[1])] < pl[u]

    with ExitStack() as ctx:
        def sb(name, shape, dt=F32):
            return ctx.enter_context(nc.sbuf_tensor(name, shape, dt))

        def psum(name, shape):
            return ctx.enter_context(nc.psum_tensor(name, shape, F32))

        def sem(name):
            return ctx.enter_context(nc.semaphore(name))

        padded = sb("padded", [P, CT, S + 2, S + 2])
        xr = sb("xr", [P, CT, S + 1, S])
        e = sb("e", [P, CT, S // 2 + 2, S])
        Y = sb("Y", [P, CT, S, S])
        wr_sb = sb("wr_sb", [P, KT, CT * P])
        pw_sb = sb("pw_sb", [P, 2 * CT, KT * P])
        wa_sb = sb("wa_sb", [P, CT, KT * P])
        dft = sb("dft", [P, 6, P])
        ident = sb("ident", [P, P])
        ones = sb("ones", [P, P])
        tt = sb("tt", [P, TSLOTS, 1024])
        fw = sb("fw", [P, 2, CT, CH])
        sq = sb("sq", [P, 8, 2, S])
        im = sb("im", [P, 8, S])
        Z = sb("Z", [P, 8, 2, S])
        xin = sb("xin", [P, 2, KT, CH])
        res = sb("res", [P, 2, KT, CH])
        attn = sb("attn", [P, CT, P])
        rdiag = sb("rdiag", [P, CT, P])
        cscale = sb("cscale", [P, CT, P])
        gram_b = sb("gram_b", [P, CT, 32])
        gram_t = sb("gram_t", [P, CT, 32])
        scores = sb("scores", [P, CT, 32])
        expd = sb("expd", [P, CT, 32])
        dw_sb = sb("dw_sb", [P, CT, 9])
        cv = sb("cv", [P, 8, CT])
        po_b = sb("po_b", [P, KT])
        g1_sb = sb("g1_sb", [P, CT, HG])
        g2_sb = sb("g2_sb", [HG, CT * P])
        gb1 = sb("gb1", [HG, 1])
        hid = sb("hid", [HG, 1])
        bn_s = sb("bn_s", [P, CT])
        bn_b = sb("bn_b", [P, CT])
        ng_b2 = sb("ng_b2", [P, CT])
        t_a = sb("t_a", [P, CT])
        t_b = sb("t_b", [P, CT])
        sums = sb("sums", [P, CT, NCONV])
        ssq = sb("ssq", [P, CT, NCONV])
        tot = sb("tot", [P, CT])
        tsq = sb("tsq", [P, CT])
        nrm = sb("nrm", [P, CT])
        rn = sb("rn", [P, CT])
        rnt = sb("rnt", [P, CT])
        nmax = sb("nmax", [P, CT])
        esum = sb("esum", [P, CT])
        rsum = sb("rsum", [P, CT])
        gexp = sb("gexp", [P, CT])
        gplus = sb("gplus", [P, CT])
        gate = sb("gate", [P, CT])
        REDUCE_B, DW_B, BN_G, BN_BETA, BN_MEAN, BN_VAR, GATE_B2, TEMP = range(8)

        pslot = psum("pslot", [P, PSLOTS, 1024])
        pgram = psum("pgram", [P, 512])
        psmall = psum("psmall", [P, 512])

        consts_in = sem("consts_in")
        xin_full = [sem(f"xin_full{k}") for k in range(2)]
        res_full = [sem(f"res_full{k}") for k in range(2)]
        stored = [sem(f"stored{k}") for k in range(2)]
        cleared = sem("cleared")
        prep_act = sem("prep_act")
        prep_dve = sem("prep_dve")
        filled = sem("filled")
        emptied = [sem(f"emptied{k}") for k in range(PSLOTS)]
        gram_sums = sem("gram_sums")
        gate_mm = sem("gate_mm")
        sq_ready = sem("sq_ready")
        z_re = sem("z_re")
        centred = sem("centred")
        tapped = sem("tapped")
        relu_done = sem("relu_done")
        stats = sem("stats")
        wrapped = sem("wrapped")
        e_ready = sem("e_ready")
        mirrored = sem("mirrored")
        small = sem("small")
        nrm_ready = sem("nrm_ready")
        hid_ready = sem("hid_ready")
        gexp_ready = sem("gexp_ready")
        exp_ready = sem("exp_ready")

        def position(u, b, last):
            return PRE + (place_last if last else place)[u] + PER * b

        def slot(u, last):
            return (PRE + (place_last if last else place)[u]) % PSLOTS

        def wait_filled(eng, u, b, last=False):
            eng.wait_ge(filled, position(u, b, last) + 1)

        def wait_emptied(eng, u, b, last=False):
            n = PRE + (place_last if last else place)[u]
            eng.wait_ge(emptied[n % PSLOTS], n // PSLOTS + 1 + (PER // PSLOTS) * b)

        block = ctx.enter_context(nc.Block())

        def conv_view(ct, j, tap):
            dy, dx = tap // 3, tap % 3
            r = CONV_ROWS * j + dy
            return padded[:, ct, r:r + CONV_ROWS, dx:dx + S]

        def conv_out(ct, j):
            return xr[:, ct, CONV_ROWS * j:CONV_ROWS * (j + 1), 0:S]

        SMALL_STEPS = {}
        SMALL_NAMES = ["tot", "tsq", "nmaxed", "rn", "rnt", "rdiag0", "rdiag", "gplus", "gate",
                       "scores", "nmax", "rsum", "attn"]
        SMALL_WEIGHTS = [1, 1, 1, 1, 1, 1, 1, 1, 1, 19, 1, 1, 8]
        at = 0
        for name, w in zip(SMALL_NAMES, SMALL_WEIGHTS):
            at += w
            SMALL_STEPS[name] = at
        SMALL_PER = at

        def small_at(name, b):
            return SMALL_STEPS[name] + SMALL_PER * b

        E_PER = 2 * CT
        MIRRORED_PER = 5 * CT

        def mirrored_at(i):
            return MIRRORED_PER // CT * (i // 4) + (2, 3, 5)[i % 4]

        Z_RE_PER = 10

        def z_re_at(i):
            return i + 1 + (1 if i < 4 else 2)

        @block.sync
        def _(sp):
            for dst, src in ((wr_sb, reduce_wt), (dw_sb, dw), (cv, channel), (po_b, bias_out),
                             (g1_sb, gate_w1t), (g2_sb, gate_w2t), (gb1, gate_b1), (pw_sb, post_wt),
                             (dft, fourier), (ident, identity)):
                sp.dma_start(dst[:], src).then_inc(consts_in, 16)

            def pixels(t, b, start, n):
                return t[b].rearrange("(t p) h w -> p t (h w)", p=P)[:, :, start:start + n]

            def load_x(b, k):
                sp.dma_start(xin[:, k % 2], pixels(x, b, CH * k, CH)).then_inc(xin_full[k % 2], 16)

            HALF = CH // 2
            LOWER = S * S // 2

            def load_res(b, k):
                for a in range(2):
                    sp.dma_start(res[:, k % 2, :, HALF * a:HALF * (a + 1)],
                                 pixels(x, b, HALF * k + LOWER * a, HALF)).then_inc(res_full[k % 2], 16)

            for k in range(NCH):
                if k >= 2:
                    sp.wait_ge(filled, k - 1)
                load_x(0, k)

            def batch(b, last):
                if not last:
                    load_x(b + 1, 0)
                    load_x(b + 1, 1)
                if not last:
                    for k in range(2, NCH):
                        wait_filled(sp, ("A", k - 2), b)
                        load_x(b + 1, k)
                for k in range(NCH):
                    wait_emptied(sp, ("P1", k), b, last)
                    for a in range(2):
                        sp.dma_start(pixels(out, b, HALF * k + LOWER * a, HALF),
                                     res[:, k % 2, :, HALF * a:HALF * (a + 1)]).then_inc(stored[k % 2], 16)
                    if k >= 1 and k + 1 < NCH:
                        sp.wait_ge(stored[(k - 1) % 2], 32 * ((k - 1) // 2 + 1) + 32 * (NCH // 2) * b)
                        load_res(b, k + 1)
                for k in range(2):
                    sp.wait_ge(stored[k], 32 * (NCH // 2) + 32 * (NCH // 2) * b)
                    if not last:
                        load_res(b + 1, k)

            sp.wait_ge(filled, NCH)
            for k in range(2):
                load_res(0, k)
            with sp.Fori(0, B - 1) as b:
                batch(b, False)
            batch(B - 1, True)

        @block.gpsimd
        def _(pool):
            nc.gpsimd.memset(padded[:, :, 0:S + 2:S + 1, :], 0.0).then_inc(cleared, 1)
            nc.gpsimd.memset(padded[:, :, 1:S + 1, 0:S + 2:S + 1], 0.0).then_inc(cleared, 1)
            nc.gpsimd.memset(attn[:], 0.0).then_inc(cleared, 1)
            nc.gpsimd.memset(ones[:], 1.0).then_inc(cleared, 1)

        @block.tensor
        def _(pe):
            pe.wait_ge(consts_in, 160)
            pe.wait_ge(cleared, 4)

            def reduce_chunk(k, slot_k, x_count):
                pe.wait_ge(xin_full[k % 2], x_count)
                for m in range(CT):
                    for t in range(KT):
                        mm = nc.tensor.matmul(pslot[:, slot_k, CH * m:CH * (m + 1)],
                                              wr_sb[:, t, P * m:P * (m + 1)], xin[:, k % 2, t, :],
                                              start=(t == 0), stop=(t == KT - 1))
                mm.then_inc(filled, 1)

            for k in range(NCH):
                if k >= PSLOTS:
                    pe.wait_ge(emptied[k % PSLOTS], k // PSLOTS)
                reduce_chunk(k, k % PSLOTS, 16 * (k // 2 + 1))

            def rows_of(image, ct, row, n):
                return image[:, ct].rearrange("p h w -> p (h w)")[:, S * row:S * (row + n)]

            def batch(b, last):
                pl = place_last if last else place

                def begin(u, *sources):
                    n = PRE + pl[u]
                    need = {n % PSLOTS: n // PSLOTS}
                    for v in sources:
                        m = PRE + pl[v]
                        need[m % PSLOTS] = max(need.get(m % PSLOTS, 0), m // PSLOTS + 1)
                    for k in sorted(need):
                        pe.wait_ge(emptied[k], need[k] + (PER // PSLOTS) * b)
                    return n % PSLOTS

                def transposes(u, part, tiles=8, sources=()):
                    k = begin(u, *sources)
                    for n in range(tiles):
                        t = nc.tensor.transpose(pslot[:, k, P * n:P * (n + 1)], part(n), ident[:])
                    t.then_inc(filled, 1)

                def transform(u, source, matrix):
                    ts = transposed[source] % TSLOTS
                    k = begin(u, source)
                    for n in range(8):
                        mm = nc.tensor.matmul(pslot[:, k, P * n:P * (n + 1)], tt[:, ts, P * n:P * (n + 1)],
                                              dft[:, matrix(n), :], start=(n % 4 == 0), stop=True,
                                              skip_group_check=True)
                    mm.then_inc(filled, 1)

                for u in (order_last if last else order):
                    kind, i = u
                    ct, q = i // 4, i % 4
                    if kind == "A":
                        reduce_chunk(i, begin(u), 16 * (i // 2 + 1) + 16 * (NCH // 2) * (b + 1))
                    elif kind == "CS":
                        pe.wait_ge(small, small_at("tot", b))
                        for t in range(CT):
                            mm = nc.tensor.matmul(psmall[0:HG, 0:1], g1_sb[:, t, :], tot[:, t:t + 1],
                                                  start=(t == 0), stop=(t == CT - 1))
                        mm.then_inc(gate_mm, 1)
                        pe.wait_ge(small, small_at("rdiag", b))
                        k = begin(u)
                        mm = nc.tensor.matmul(pslot[:, k, 0:CT * P], ones[:], rdiag[:].rearrange("p a b -> p (a b)"),
                                              start=True, stop=True)
                        mm.then_inc(filled, 1)
                    elif kind == "T1":
                        if i == 0:
                            pe.wait_ge(relu_done, NCONV * CT * (b + 1))
                        transposes(u, lambda n: rows_of(xr, ct, 16 * q + 2 * n, 2))
                    elif kind == "R1":
                        if i == 0:
                            pe.wait_ge(e_ready, E_PER * (b + 1))
                        transposes(u, lambda n: rows_of(e, ct, 16 * q + 2 * n, 2), 8 if q < 2 else 1)
                    elif kind == "D1":
                        if q < 3:
                            ta = transposed[("T1", i)] % TSLOTS
                            pe.wait_ge(mirrored, mirrored_at(i) + MIRRORED_PER * b)
                            tb = transposed[("R1", i)] % TSLOTS
                            for n in range(8 if q < 2 else 1):
                                rows = slice(0, P if q < 2 else S)
                                mm = nc.tensor.matmul(pgram[:, P * ct:P * (ct + 1)], tt[rows, ta, P * n:P * (n + 1)],
                                                      tt[rows, tb, P * n:P * (n + 1)], start=(i == 0 and n == 0),
                                                      stop=(q == 2), skip_group_check=True)
                            if i == 6:
                                mm.then_inc(gram_sums, 1)
                        transform(u, ("T1", i), lambda n: D1)
                    elif kind == "T2":
                        transposes(u, lambda n: rows_of(Y, ct, 16 * q + 2 * n, 2), sources=[("D1", 4 * ct + 3)])
                        if i == 1:
                            pe.wait_ge(hid_ready, b + 1)
                            for t in range(CT):
                                mm = nc.tensor.matmul(psmall[:, 1 + t:2 + t], g2_sb[:, P * t:P * (t + 1)], hid[:],
                                                      start=True, stop=True)
                            mm.then_inc(gate_mm, 1)
                    elif kind == "D2":
                        transform(u, ("T2", i), lambda n: D2S if q == 0 and n == 0 else D2)
                    elif kind == "T3":
                        pe.wait_ge(z_re, z_re_at(i) + Z_RE_PER * b)
                        transposes(u, lambda n: Z[:, n].rearrange("p r k -> p (r k)"), sources=[("D2", i)])
                    elif kind == "D3":
                        transform(u, ("T3", i), lambda n: D3S if q == 0 and n == 0 else D3)
                    elif kind == "W":
                        pe.wait_ge(small, small_at("attn", b))
                        k = begin(u)
                        for t in range(CT):
                            mm = nc.tensor.matmul(pslot[:, k, 512 * t:512 * t + KT * P], attn[:, t, :],
                                                  pw_sb[:, t, :], start=True, stop=True)
                        mm.then_inc(filled, 1)
                    elif kind == "T4":
                        transposes(u, lambda n: Y[:, n // 4].rearrange("p k h -> p (k h)")[:, 4 * i + n % 4::32],
                                   sources=[("D3", 7)])
                    elif kind == "D4":
                        transform(u, ("T4", i), lambda n: D4)
                    else:
                        half = int(kind[1])
                        k = begin(u, ("D4", i), ("W", 0))
                        for m in range(2):
                            o = 2 * half + m
                            dst = pslot[:, k, CH * m:CH * (m + 1)]
                            for t in range(CT):
                                mm = nc.tensor.matmul(dst, pw_sb[:, CT + t, P * o:P * (o + 1)], fw[:, i % 2, t, :],
                                                      start=(t == 0), stop=False, skip_group_check=True)
                            for t in range(CT):
                                w = wa_sb[:, t, P * o:P * (o + 1)]
                                nc.tensor.matmul(dst[:, 0:CH // 2], w, rows_of(e, t, 4 * i, 4), start=False,
                                                 stop=(t == CT - 1), skip_group_check=True)
                                low = dst[:, CH // 2:CH].rearrange("p (h w) -> p h w", w=S)
                                r = S // 2 - 4 * i
                                nc.tensor.matmul(low[:, :, 1:S], w, e[:, t, r:r - 4:-1, S - 1:0:-1], start=False,
                                                 stop=(t == CT - 1), skip_group_check=True)
                                mm = nc.tensor.matmul(low[:, :, 0], w, e[:, t, r:r - 4:-1, 0], start=False,
                                                      stop=(t == CT - 1), skip_group_check=True)
                        mm.then_inc(filled, 1)

            with pe.Fori(0, B - 1) as b:
                batch(b, False)
            batch(B - 1, True)

        @block.scalar
        def _(act):
            act.wait_ge(consts_in, 160)
            act.wait_ge(prep_dve, 1)
            nc.scalar.activation(t_b[:], t_a[:], ACT.Sqrt).then_inc(prep_act, 1)
            act.wait_ge(cleared, 4)

            def pad_chunk(k, slot_k):
                for m in range(CT):
                    a = nc.scalar.activation(
                        padded[:, m, 1 + 8 * k:9 + 8 * k, 1:S + 1],
                        pslot[:, slot_k, CH * m:CH * (m + 1)].rearrange("p (h w) -> p h w", w=S),
                        ACT.Identity, bias=cv[:, REDUCE_B, m:m + 1])
                a.then_inc(emptied[slot_k], 1)

            def centre(j):
                for t in range(CT):
                    nc.scalar.activation(conv_out(t, j), conv_view(t, j, 4), ACT.Copy,
                                         scale=dw_sb[:, t, 4:5]).then_inc(centred, 1)

            def relu(j, base):
                act.wait_ge(tapped, CONV_OPS * (j + 1) + base)
                for t in range(CT):
                    nc.scalar.activation(conv_out(t, j), conv_out(t, j), ACT.Relu, scale=bn_s[:, t:t + 1],
                                         bias=bn_b[:, t:t + 1], accum_out=sums[:, t, j:j + 1]).then_inc(relu_done, 1)

            def squares(j, base):
                act.wait_ge(relu_done, CT * (j + 1) + base)
                for t in range(CT):
                    if not (isinstance(base, int) and base + CT * j + t == 0):
                        act.wait_ge(stats, CT * j + t + base)
                    nc.scalar.activation(sq[:].rearrange("p a b c -> p (a b c)").rearrange("p (h w) -> p h w", w=S),
                                         conv_out(t, j), ACT.Square, accum_out=ssq[:, t, j:j + 1]).then_inc(stats, 1)

            for k in range(NCH):
                act.wait_ge(filled, k + 1)
                pad_chunk(k, k % PSLOTS)
                act.wait_ge(emptied[k % PSLOTS], k // PSLOTS + 1)
                if k % 2 == 1:
                    centre(k // 2)
            act.wait_ge(prep_dve, 4)
            for j in range(NCONV):
                relu(j, 0)
                squares(j, 0)

            def batch(b, last):
                wait = lambda u: wait_filled(act, u, b, last)
                done_taps = CONV_OPS * NCONV * (b + 1)
                done_relu = NCONV * CT * (b + 1)

                def copy_tile(u):
                    k = slot(u, last)
                    nc.scalar.activation(tt[:, transposed[u] % TSLOTS, :], pslot[:, k, :],
                                         ACT.Copy).then_inc(emptied[k], 1)

                for u in (order_last if last else order):
                    kind, i = u
                    ct, q = i // 4, i % 4
                    if kind in ("CS", "T3", "R1"):
                        if kind == "CS":
                            act.wait_ge(small, small_at("tsq", b))
                            nc.scalar.activation(nrm[:], tsq[:], ACT.Sqrt).then_inc(nrm_ready, 1)
                            act.wait_ge(gate_mm, 1 + 2 * b)
                            nc.scalar.activation(hid[:], psmall[0:HG, 0:1], ACT.Relu, bias=gb1[:],
                                                 scale=1.0 / (S * S)).then_inc(hid_ready, 1)
                        continue
                    if kind == "P0":
                        if not last:
                            if i == 0:
                                for c in range(NCH):
                                    wait_emptied(act, ("A", c), b)
                                centre(0)
                                centre(1)
                                centre(2)
                                centre(3)
                            if i in (2, 4, 5, 7):
                                j = (2, 4, 5, 7).index(i)
                                relu(j, done_taps)
                                squares(j, done_relu)
                        continue
                    if kind == "P1":
                        continue
                    wait(u)
                    k = slot(u, last)
                    if kind in ("T1", "T2", "T4"):
                        copy_tile(u)
                    elif kind == "A":
                        pad_chunk(i, k)
                    elif kind == "D1":
                        dst = Y[:, ct, :, 16 * q:16 * q + 16].rearrange("p k (n a) -> p k n a", a=2)
                        src = pslot[:, k, :].rearrange("p (n k a) -> p k n a", n=8, a=2)
                        nc.scalar.activation(dst, src, ACT.Copy).then_inc(emptied[k], 1)
                    elif kind == "D2":
                        v = pslot[:, k, :].rearrange("p (n r k) -> p n r k", n=8, r=2)
                        if i == 0:
                            act.wait_ge(stats, NCONV * CT * (b + 1))
                        if i >= 1:
                            act.wait_ge(z_re, z_re_at(i - 1) + Z_RE_PER * b)
                            wait_emptied(act, ("D2", i - 1), b, last)
                        nc.scalar.activation(sq[:], v, ACT.Square)
                        nc.scalar.activation(im[:], v[:, :, 1, :], ACT.Copy).then_inc(sq_ready, 1)
                        if i == 1:
                            act.wait_ge(gate_mm, 2 + 2 * b)
                            for t in range(CT):
                                a = nc.scalar.activation(gexp[:, t:t + 1], psmall[:, 1 + t:2 + t], ACT.Exp,
                                                         scale=-1.0, bias=ng_b2[:, t:t + 1])
                            a.then_inc(gexp_ready, 1)
                        if i == 3:
                            act.wait_ge(small, small_at("nmax", b))
                            for t in range(CT):
                                a = nc.scalar.activation(expd[:, t, :], scores[:, t, :], ACT.Exp,
                                                         bias=nmax[:, t:t + 1], accum_out=esum[:, t:t + 1])
                                a.then_inc(exp_ready, 1)
                    elif kind == "D3":
                        dst = Y[:, ct, 16 * q:16 * q + 16, :].rearrange("p k h -> p (k h)")
                        nc.scalar.activation(dst, pslot[:, k, :], ACT.Copy).then_inc(emptied[k], 1)
                    elif kind == "W":
                        nc.scalar.activation(wa_sb[:].rearrange("p a b -> p (a b)"), pslot[:, k, :], ACT.Copy,
                                             scale=0.5).then_inc(emptied[k], 1)
                    elif kind == "D4":
                        if i == 0:
                            act.wait_ge(small, small_at("gate", b))
                        for t in range(CT):
                            a = nc.scalar.activation(
                                fw[:, i % 2, t, :].rearrange("p (a g w) -> p g a w", a=2, g=4),
                                pslot[:, k, CH * t:CH * (t + 1)].rearrange("p (g a w) -> p g a w", g=4, a=2),
                                ACT.Copy, scale=gate[:, t:t + 1])
                        a.then_inc(emptied[k], 1)

            with act.Fori(0, B - 1) as b:
                batch(b, False)
            batch(B - 1, True)

        @block.vector
        def _(dve):
            dve.wait_ge(consts_in, 160)
            nc.vector.tensor_scalar(t_a[:], cv[:, BN_VAR, :], BN_EPS, None, ALU.add).then_inc(prep_dve, 1)
            nc.vector.tensor_scalar(ng_b2[:], cv[:, GATE_B2, :], -1.0, None, ALU.mult)
            dve.wait_ge(prep_act, 1)
            nc.vector.reciprocal(rn[:], t_b[:]).then_inc(prep_dve, 1)
            dve.wait_ge(prep_dve, 2)
            nc.vector.tensor_tensor(bn_s[:], cv[:, BN_G, :], rn[:], ALU.mult).then_inc(prep_dve, 1)
            nc.vector.tensor_tensor(nrm[:], cv[:, DW_B, :], cv[:, BN_MEAN, :], ALU.subtract)
            dve.drain()
            nc.vector.tensor_tensor(rnt[:], nrm[:], bn_s[:], ALU.mult)
            dve.drain()
            nc.vector.tensor_tensor(bn_b[:], rnt[:], cv[:, BN_BETA, :], ALU.add).then_inc(prep_dve, 1)

            def conv_step(n, base, centre_base, chunks=None):
                j, tap, t = n // CONV_OPS, TAPS[n % CONV_OPS // CT], n % CT
                if n % CONV_OPS == 0:
                    dve.wait_ge(centred, CT * (j + 1) + centre_base)
                    if chunks is not None:
                        c = min(2 * j + 2, NCH - 1)
                        dve.wait_ge(emptied[c % PSLOTS], c // PSLOTS + 1)
                if n >= CT:
                    dve.wait_ge(tapped, n - CT + 1 + base)
                nc.vector.scalar_tensor_tensor(out=conv_out(t, j), in0=conv_view(t, j, tap),
                                               scalar=dw_sb[:, t, tap:tap + 1], in1=conv_out(t, j),
                                               op0=ALU.mult, op1=ALU.add).then_inc(tapped, 1)

            for n in range(CONV_OPS * NCONV):
                conv_step(n, 0, 0, chunks=True)

            def batch(b, last):
                wait = lambda u: wait_filled(dve, u, b, last)
                count = [0]
                conv_base = CONV_OPS * NCONV * (b + 1)
                centre_base = CT * NCONV * (b + 1)

                def step(ins, name=None):
                    count[0] += 1
                    ins.then_inc(small, 1)
                    if name is not None:
                        assert SMALL_STEPS[name] == count[0], (name, count[0])
                    dve.wait_ge(small, count[0] + SMALL_PER * b)

                for u in (order_last if last else order):
                    kind, i = u
                    ct, q = i // 4, i % 4
                    k = slot(u, last)
                    if kind == "CS":
                        dve.wait_ge(stats, NCONV * CT * (b + 1))
                        step(nc.vector.tensor_reduce(tot[:], sums[:], AX_X, ALU.add), "tot")
                        step(nc.vector.tensor_reduce(tsq[:], ssq[:], AX_X, ALU.add), "tsq")
                        dve.wait_ge(nrm_ready, b + 1)
                        step(nc.vector.tensor_scalar(nrm[:], nrm[:], NORM_EPS, None, ALU.max))
                        step(nc.vector.reciprocal(rn[:], nrm[:]), "rn")
                        step(nc.vector.tensor_tensor(rnt[:], rn[:], cv[:, TEMP, :], ALU.mult), "rnt")
                        for t in range(CT):
                            step(nc.vector.tensor_scalar(rdiag[:, t, :], ident[:], rn[:, t:t + 1], None, ALU.mult))
                        nc.vector.tensor_copy(xr[:, :, S, :], xr[:, :, 0, :]).then_inc(wrapped, 1)
                        dve.wait_ge(wrapped, b + 1)
                        for t in range(CT):
                            nc.vector.tensor_tensor(e[:, t, :, 1:S], xr[:, t, 0:S // 2 + 2, 1:S],
                                                    xr[:, t, S:S // 2 - 2:-1, S - 1:0:-1], ALU.add).then_inc(e_ready, 1)
                            nc.vector.tensor_tensor(e[:, t, :, 0], xr[:, t, 0:S // 2 + 2, 0],
                                                    xr[:, t, S:S // 2 - 2:-1, 0], ALU.add).then_inc(e_ready, 1)
                        wait(u)
                        nc.vector.tensor_copy(cscale[:].rearrange("p a b -> p (a b)"),
                                              pslot[:, k, 0:CT * P]).then_inc(emptied[k], 1)
                    elif kind == "R1":
                        wait(u)
                        wait_emptied(dve, ("T1", i), b, last)
                        ta, tb = transposed[("T1", i)] % TSLOTS, transposed[u] % TSLOTS
                        rows, cols = (slice(0, P), slice(0, 1024)) if q < 2 else (slice(0, S), slice(0, P))
                        nc.vector.tensor_tensor(tt[rows, tb, cols], pslot[rows, k, cols], tt[rows, ta, cols],
                                                ALU.subtract).then_inc(mirrored, 1)
                        base = MIRRORED_PER // CT * ct + (0, 2, 3)[q]
                        dve.wait_ge(mirrored, base + 1 + MIRRORED_PER * b)
                        dve.sem_inc(emptied[k], 1)
                        if q != 1:
                            nc.vector.tensor_scalar(tt[0:S, tb, 0:P], tt[0:S, tb, 0:P], 0.5, None,
                                                    ALU.mult).then_inc(mirrored, 1)
                    elif kind == "D2":
                        v = pslot[:, k, :].rearrange("p (n r k) -> p n r k", n=8, r=2)
                        dve.wait_ge(sq_ready, i + 1 + 8 * b)
                        if i >= 1:
                            wait(("T3", i - 1))
                        nc.vector.tensor_tensor(Z[:, :, 0, :], sq[:, :, 0, :], sq[:, :, 1, :],
                                                ALU.subtract).then_inc(z_re, 1)
                        nc.vector.scalar_tensor_tensor(out=Z[:, :, 1, :], in0=v[:, :, 0, :], scalar=2.0, in1=im[:],
                                                       op0=ALU.mult, op1=ALU.mult).then_inc(emptied[k], 1)
                        if q == 0:
                            wait_emptied(dve, u, b, last)
                            nc.vector.tensor_copy(Z[:, 0, :, 0:S:32], sq[:, 0, :, 0:S:32]).then_inc(z_re, 1)
                        if i == 2:
                            dve.wait_ge(gexp_ready, b + 1)
                            step(nc.vector.tensor_scalar(gplus[:], gexp[:], 1.0, None, ALU.add), "gplus")
                            step(nc.vector.reciprocal(gate[:], gplus[:]), "gate")
                            dve.wait_ge(gram_sums, b + 1)
                            wait_emptied(dve, ("CS", 0), b, last)
                            for t in range(CT):
                                for g in range(4):
                                    rows = slice(32 * g, 32 * g + 32)
                                    step(nc.vector.tensor_copy(gram_b[rows, t, :],
                                                               pgram[rows, P * t + 32 * g:P * t + 32 * g + 32]))
                            for t in range(CT):
                                step(nc.vector.transpose(gram_t[:, t, :], gram_b[:, t, :]))
                            step(nc.vector.tensor_tensor(gram_b[:], gram_b[:], gram_t[:], ALU.add))
                            for t in range(CT):
                                for g in range(4):
                                    rows = slice(32 * g, 32 * g + 32)
                                    step(nc.vector.scalar_tensor_tensor(
                                        out=scores[rows, t, :], in0=gram_b[rows, t, :],
                                        scalar=rnt[rows, t:t + 1], in1=cscale[rows, t, 32 * g:32 * g + 32],
                                        op0=ALU.mult, op1=ALU.mult))
                            step(nc.vector.tensor_reduce(nmax[:], scores[:], AX_X, ALU.max, negate=True), "nmax")
                        if i == 4:
                            dve.wait_ge(exp_ready, 2 * (b + 1))
                            step(nc.vector.reciprocal(rsum[:], esum[:]), "rsum")
                            for t in range(CT):
                                for g in range(4):
                                    rows = slice(32 * g, 32 * g + 32)
                                    step(nc.vector.tensor_scalar(attn[rows, t, 32 * g:32 * g + 32], expd[rows, t, :],
                                                                 rsum[rows, t:t + 1], None, ALU.mult))
                    elif kind == "T3":
                        wait(u)
                        nc.vector.tensor_copy(tt[:, transposed[u] % TSLOTS, :], pslot[:, k, :]).then_inc(emptied[k], 1)
                    elif kind in ("P0", "P1"):
                        half = int(kind[1])
                        wait(u)
                        if half == 0:
                            dve.wait_ge(res_full[i % 2], 32 * (i // 2 + 1) + 32 * (NCH // 2) * b)
                        for m in range(2):
                            o = 2 * half + m
                            add = nc.vector.scalar_tensor_tensor(
                                out=res[:, i % 2, o, :], in0=pslot[:, k, CH * m:CH * (m + 1)],
                                scalar=po_b[:, o:o + 1], in1=res[:, i % 2, o, :],
                                op0=ALU.add, op1=ALU.add)
                        add.then_inc(emptied[k], 1)
                        if not last:
                            p = 2 * i + half
                            for n in range(CONV_PER_POST * p, min(CONV_PER_POST * (p + 1), CONV_OPS * NCONV)):
                                conv_step(n, conv_base, centre_base)
                assert count[0] == SMALL_PER, count

            with dve.Fori(0, B - 1) as b:
                batch(b, False)
            batch(B - 1, True)


_VECTORS = ["reduce_b", "dw_b", "bn_gamma", "bn_beta", "bn_mean", "bn_var", "gate_b2"]


def kernel(**inputs):
    import concourse.bacc as _bacc
    from concourse.bass_utils import run_bass_kernel_spmd as _run

    a = {k.replace("L0_conv_", ""): np.asarray(v) for k, v in inputs.items()}
    mid, cin = a["reduce_w"].shape

    def tiles(v):
        return v.reshape(-1, P).T

    def weight(w):
        return w.T.reshape(-1, P, w.shape[0]).transpose(1, 0, 2)

    temp = np.repeat(a["temperature"].reshape(-1), mid // a["temperature"].size)
    layout = {
        "x": a["x"],
        "reduce_wt": weight(a["reduce_w"]),
        "dw": a["dw_w"].reshape(-1, P, 9).transpose(1, 0, 2),
        "channel": np.stack([tiles(a[n]) for n in _VECTORS] + [tiles(temp)], axis=1),
        "bias_out": tiles(a["post_b"]),
        "gate_w1t": weight(a["gate_w1"]),
        "gate_b1": a["gate_b1"].reshape(-1, 1),
        "gate_w2t": a["gate_w2"].T,
        "post_wt": weight(a["post_w"]),
        "fourier": fourier_matrices(),
        "identity": np.eye(P, dtype=np.float32),
    }
    nc = _bacc.Bacc("TRN2", target_bir_lowering=False, num_devices=1)
    arrays, args = {}, {}
    for name, v in layout.items():
        v = np.ascontiguousarray(v)
        arrays[f"in_{name}"] = v
        args[name] = nc.dram_tensor(f"in_{name}", v.shape, mybir.dt.from_np(v.dtype), kind="ExternalInput").ap()
    out = nc.dram_tensor("out_y", a["x"].shape, F32, kind="ExternalOutput").ap()
    build(nc, out=out, **args)
    r = _run(nc, [arrays], core_ids=[0])
    return r.results[0]["out_y"]
```

```python
from contextlib import ExitStack

import numpy as np

import concourse.bass as bass
from concourse import mybir


F32 = mybir.dt.float32
F32R = mybir.dt.float32r
ALU = mybir.AluOpType
ACT = mybir.ActivationFunctionType
AX_X = mybir.AxisListType.X

P = 128
S = 64
CH = 512
NCH = S * S // CH
BN_EPS = 1e-5
NORM_EPS = 1e-12
TAPS = [0, 1, 2, 3, 5, 6, 7, 8]
CONV_ROWS = 16
NCONV = S // CONV_ROWS
CONV_OPS = len(TAPS) * 2
CONV_EARLY = 16
CONV_PER_POST = [4, 3]
TSLOTS = 4
PSLOTS = 3


def fourier_matrices():
    n = np.arange(S)
    ang = 2 * np.pi * np.outer(n, n) / S
    c, s = np.cos(ang) / 8, np.sin(ang) / 8
    eye2 = np.eye(2)
    alt = (-1.0) ** n / 8
    row = np.stack([c[:, :32], -s[:, :32]], axis=2)
    row[:, 0, 0], row[:, 0, 1] = 1 / 8, alt
    d1 = np.einsum("wkr,ab->awkrb", row, eye2).reshape(P, P)
    d2 = np.block([[c, -s], [s, c]])
    lane = np.zeros((2, S, 2, S))
    for r in range(2):
        lane[r, :, 0, 32 * r:32 * r + 32] = row[:, :, 0]
        lane[r, :, 1, 32 * r:32 * r + 32] = row[:, :, 1]
    lane[0, :, :, 0] = row[:, 0, :]
    d2s = lane.reshape(P, P)
    d3 = np.block([[c, s], [-s, c]])
    back = np.stack([2 * c[:32, :], -2 * s[:32, :]], axis=1)
    back[0, 0, :], back[0, 1, :] = 1 / 8, alt
    unlane = np.zeros((2, S, 2, S))
    for r in range(2):
        unlane[0, 32 * r:32 * r + 32, r, :] = back[:, 0, :]
        unlane[1, 32 * r:32 * r + 32, r, :] = back[:, 1, :]
    d3s = unlane.reshape(P, P)
    d4 = np.einsum("krw,ab->krabw", back, eye2).reshape(P, P)
    return np.stack([d1, d2, d2s, d3, d3s, d4], axis=1).astype(np.float32)


D1, D2, D2S, D3, D3S, D4 = range(6)


def conv_before(p):
    return min(CONV_EARLY + sum(CONV_PER_POST[n % 2] for n in range(p)), CONV_OPS * NCONV)


def unit_order(with_next):
    order = [("CS", 0), ("T1", 0), ("R1", 0)]
    next_chunk = 0

    def reduce_next():
        nonlocal next_chunk
        if with_next:
            order.append(("A", next_chunk))
        next_chunk += 1

    for i in range(1, 8):
        order.append(("T1", i))
        order.append(("D1", i - 1))
        if i % 4 < 3:
            order.append(("R1", i))
        if i in (2, 4, 6):
            reduce_next()
    order += [("D1", 7)]
    for j in range(8 + 3):
        if j < 8:
            order.append(("T2", j))
        if 1 <= j < 9:
            order.append(("D2", j - 1))
        if 2 <= j < 10:
            order.append(("T3", j - 2))
        if 3 <= j:
            order.append(("D3", j - 3))
        if j in (1, 3, 6, 9):
            reduce_next()
    order += [("W", 0), ("T4", 0), ("T4", 1)]
    reduce_next()
    order += [("D4", 0)]
    for i in range(8):
        if 1 <= i < 7:
            order.append(("T4", i + 1))
        order.append(("P0", i))
        if i + 1 < 8:
            order.append(("D4", i + 1))
        order.append(("P1", i))
    assert next_chunk == NCH
    return order


def build(nc, x, reduce_wt, dw, channel, bias_out, gate_w1t, gate_b1, gate_w2t, post_wt, fourier, identity, out):
    B = x.shape[0]
    KT = x.shape[1] // P
    CT = reduce_wt.shape[2] // P
    HG = gate_w1t.shape[2]

    order, order_last = unit_order(True), unit_order(False)
    PRE = NCH
    PER = len(order)
    assert PER % PSLOTS == 0
    place = {u: n for n, u in enumerate(order)}
    place_last = {u: n for n, u in enumerate(order_last)}
    transposed = {u: n for n, u in enumerate([u for u in order if u[0] in ("T1", "R1", "T2", "T3", "T4")])}
    used_by = {"T1": "D1", "R1": "D1", "T2": "D2", "T3": "D3", "T4": "D4"}
    made = list(transposed)
    for n, u in enumerate(made):
        if n >= TSLOTS:
            v = made[n - TSLOTS]
            for pl in (place, place_last):
                assert pl[(used_by[v[0]], v[1])] < pl[u]

    with ExitStack() as ctx:
        def sb(name, shape, dt=F32):
            return ctx.enter_context(nc.sbuf_tensor(name, shape, dt))

        def psum(name, shape):
            return ctx.enter_context(nc.psum_tensor(name, shape, F32))

        def sem(name):
            return ctx.enter_context(nc.semaphore(name))

        padded = sb("padded", [P, CT, S + 2, S + 2])
        xr = sb("xr", [P, CT, S + 1, S])
        EW = (S // 2 + 1) * S + 2
        eh = sb("eh", [P, CT, EW], F32R)
        el = sb("el", [P, CT, EW], F32R)
        Y = sb("Y", [P, CT, S, S])
        wrh = sb("wrh", [P, KT, CT * P], F32R)
        wrl = sb("wrl", [P, KT, CT * P], F32R)
        pw1 = sb("pw1", [P, CT, KT * P])
        pwh = sb("pwh", [P, CT, KT * P], F32R)
        pwl = sb("pwl", [P, CT, KT * P], F32R)
        wah = sb("wah", [P, CT, KT * P], F32R)
        wal = sb("wal", [P, CT, KT * P], F32R)
        dft = sb("dft", [P, 6, P])
        ident = sb("ident", [P, P])
        ones = sb("ones", [P, P])
        tt = sb("tt", [P, TSLOTS, 1024])
        fxh = sb("fxh", [P, 2 * CT, CH], F32R)
        fxl = sb("fxl", [P, 2 * CT, CH], F32R)
        packed = sb("packed", [P, 2, 2])
        Z = sb("Z", [P, 8, 3, S])
        xs = sb("xs", [P, 2, KT, CH])
        edge = sb("edge", [P, CT, S // 2])
        z0 = sb("z0", [P, KT, S // 2])
        attn = sb("attn", [P, CT, P])
        rdiag = sb("rdiag", [P, CT, P])
        cscale = rdiag
        gram_b = sb("gram_b", [P, CT, 32])
        gram_t = sb("gram_t", [P, CT, 32])
        scores = sb("scores", [P, CT, 32])
        expd = sb("expd", [P, CT, 32])
        dw_sb = sb("dw_sb", [P, CT, 9])
        cv = sb("cv", [P, 8, CT])
        po_b = sb("po_b", [P, KT])
        g1_sb = sb("g1_sb", [P, CT, HG])
        g2_sb = sb("g2_sb", [HG, CT * P])
        gb1 = sb("gb1", [HG, 1])
        hid = sb("hid", [HG, 1])
        bn_s = sb("bn_s", [P, CT])
        bn_b = sb("bn_b", [P, CT])
        ng_b2 = sb("ng_b2", [P, CT])
        t_a = sb("t_a", [P, CT])
        t_b = sb("t_b", [P, CT])
        sums = sb("sums", [P, CT, NCONV])
        ssq = sb("ssq", [P, CT, 2 * NCONV])
        tot = sb("tot", [P, CT])
        tsq = sb("tsq", [P, CT])
        nrm = sb("nrm", [P, CT])
        rn = sb("rn", [P, CT])
        rnt = sb("rnt", [P, CT])
        nmax = sb("nmax", [P, CT])
        esum = sb("esum", [P, CT])
        rsum = sb("rsum", [P, CT])
        gexp = sb("gexp", [P, CT])
        gplus = sb("gplus", [P, CT])
        gate = sb("gate", [P, CT])
        REDUCE_B, DW_B, BN_G, BN_BETA, BN_MEAN, BN_VAR, GATE_B2, TEMP = range(8)

        wr_raw = tt[:, 0].rearrange("p (t n) -> p t n", t=KT)
        pw_raw = tt[:, 1].rearrange("p (t n) -> p t n", t=CT)

        pslot = psum("pslot", [P, PSLOTS, 1024])
        pgram = psum("pgram", [P, 512])
        psmall = psum("psmall", [P, 512])

        consts_in = sem("consts_in")
        xs_full = [sem(f"xs_full{k}") for k in range(2)]
        res_full = [[sem(f"res_full{h}{k}") for k in range(2)] for h in range(2)]
        stored = [[sem(f"stored{h}{k}") for k in range(2)] for h in range(2)]
        cleared = sem("cleared")
        prep_act = sem("prep_act")
        prep_dve = sem("prep_dve")
        filled = sem("filled")
        emptied = [sem(f"emptied{k}") for k in range(PSLOTS)]
        gate_mm = sem("gate_mm")
        packed_sq = sem("packed_sq")
        sq_ready = sem("sq_ready")
        z_im = sem("z_im")
        z_done = sem("z_done")
        z_re = sem("z_re")
        centred = sem("centred")
        tapped = sem("tapped")
        relu_done = sem("relu_done")
        stats = sem("stats")
        wrapped = sem("wrapped")
        e_sum = sem("e_sum")
        e_high = sem("e_high")
        e_low = sem("e_low")
        x_high = sem("x_high")
        x_low = sem("x_low")
        w_high = sem("w_high")
        f_high = sem("f_high")
        edge_ready = sem("edge_ready")
        edge_mm = sem("edge_mm")
        edge_out = sem("edge_out")
        edge_added = sem("edge_added")
        mirrored = sem("mirrored")
        small = sem("small")
        nrm_ready = sem("nrm_ready")
        hid_ready = sem("hid_ready")
        gexp_ready = sem("gexp_ready")
        exp_ready = sem("exp_ready")

        def position(u, b, last):
            return PRE + (place_last if last else place)[u] + PER * b

        def slot(u, last):
            return (PRE + (place_last if last else place)[u]) % PSLOTS

        def wait_filled(eng, u, b, last=False):
            eng.wait_ge(filled, position(u, b, last) + 1)

        def wait_emptied(eng, u, b, last=False):
            n = PRE + (place_last if last else place)[u]
            eng.wait_ge(emptied[n % PSLOTS], n // PSLOTS + 1 + (PER // PSLOTS) * b)

        block = ctx.enter_context(nc.Block())

        def conv_view(ct, j, tap):
            dy, dx = tap // 3, tap % 3
            r = CONV_ROWS * j + dy
            return padded[:, ct, r:r + CONV_ROWS, dx:dx + S]

        def conv_out(ct, j):
            return xr[:, ct, CONV_ROWS * j:CONV_ROWS * (j + 1), 0:S]

        SMALL_STEPS = {}
        SMALL_NAMES = ["tot", "tsq", "nmaxed", "rn", "rnt", "rdiag0", "rdiag", "edge0", "edge1", "gplus", "gate",
                       "scores", "nmax", "rsum", "attn"]
        SMALL_WEIGHTS = [1, 1, 1, 1, 1, 1, 1, 1, 1, 1, 1, 19, 1, 1, 8]
        at = 0
        for name, w in zip(SMALL_NAMES, SMALL_WEIGHTS):
            at += w
            SMALL_STEPS[name] = at
        SMALL_PER = at

        def small_at(name, b):
            return SMALL_STEPS[name] + SMALL_PER * b

        E_PER = 2 * 3 * CT
        MIRRORED_PER = 5 * CT

        def mirrored_at(i):
            return MIRRORED_PER // CT * (i // 4) + (2, 3, 5)[i % 4]

        XS_PER = 16 * (NCH // 2)
        RES_PER = 32 * (NCH // 2)

        @block.sync
        def _(sp):
            for dst, src in ((wr_raw, reduce_wt), (dw_sb[:], dw), (cv[:], channel), (po_b[:], bias_out),
                             (g1_sb[:], gate_w1t), (g2_sb[:], gate_w2t), (gb1[:], gate_b1),
                             (pw1[:], post_wt[:, 0:CT]), (pw_raw, post_wt[:, CT:2 * CT]),
                             (dft[:], fourier), (ident[:], identity)):
                sp.dma_start(dst, src).then_inc(consts_in, 16)

            def pixels(t, b, start, n):
                return t[b].rearrange("(t p) h w -> p t (h w)", p=P)[:, :, start:start + n]

            def load_x(b, k):
                sp.dma_start(xs[:, k % 2], pixels(x, b, CH * k, CH)).then_inc(xs_full[k % 2], 16)

            HALF = CH // 2
            LOWER = S * S // 2

            def rows(t, b, k, half, a):
                return pixels(t, b, HALF * k + LOWER * a, HALF)[:, 2 * half:2 * half + 2]

            def summed(k, half, a):
                return xs[:, k % 2, 2 * half:2 * half + 2, HALF * a:HALF * (a + 1)]

            def load_res(b, k, half):
                for a in range(2):
                    sp.dma_start(summed(k, half, a), rows(x, b, k, half, a)).then_inc(res_full[half][k % 2], 16)

            for k in range(NCH):
                if k >= 2:
                    sp.wait_ge(x_low, k - 1)
                load_x(0, k)

            def batch(b, last, more):
                if not last:
                    for k in range(2, NCH):
                        sp.wait_ge(x_low, k - 1 + NCH * (b + 1))
                        load_x(b + 1, k)
                    for k in range(2):
                        sp.wait_ge(x_low, NCH - 1 + k + NCH * (b + 1))
                        for half in range(2):
                            load_res(b, k, half)
                for k in range(NCH):
                    for half in range(2):
                        wait_emptied(sp, (f"P{half}", k), b, last)
                        for a in range(2):
                            sp.dma_start(rows(out, b, k, half, a),
                                         summed(k, half, a)).then_inc(stored[half][k % 2], 16)
                        n = 2 * k + half - 1
                        if n >= 0 and n // 2 + 2 < NCH:
                            kb, hb = n // 2, n % 2
                            sp.wait_ge(stored[hb][kb % 2], 32 * (kb // 2 + 1) + RES_PER * b)
                            load_res(b, kb + 2, hb)
                for k in range(2):
                    for half in range(2):
                        sp.wait_ge(stored[half][k], RES_PER * (b + 1))
                    if more:
                        load_x(b + 2, k)

            for k in range(2):
                sp.wait_ge(x_low, NCH - 1 + k)
                load_x(1, k)
            with sp.Fori(0, B - 2) as b:
                batch(b, False, True)
            batch(B - 2, False, False)
            for k in range(2):
                for half in range(2):
                    load_res(B - 1, k, half)
            batch(B - 1, True, False)

        @block.gpsimd
        def _(pool):
            nc.gpsimd.memset(padded[:, :, 0:S + 2:S + 1, :], 0.0).then_inc(cleared, 1)
            nc.gpsimd.memset(padded[:, :, 1:S + 1, 0:S + 2:S + 1], 0.0).then_inc(cleared, 1)
            nc.gpsimd.memset(attn[:], 0.0).then_inc(cleared, 1)
            nc.gpsimd.memset(ones[:], 1.0).then_inc(cleared, 1)

        @block.tensor
        def _(pe):
            pe.wait_ge(consts_in, 16 * 11)
            pe.wait_ge(cleared, 4)

            def split_product(dst, w, v, first=True, last=True):
                for n, (a, c) in enumerate(((0, 0), (0, 1), (1, 0))):
                    mm = nc.tensor.matmul(dst, w[a], v[c], start=first and n == 0, stop=last and n == 2,
                                          skip_group_check=True)
                return mm

            def reduce_chunk(k, slot_k, x_count):
                pe.wait_ge(x_low, x_count)
                for m in range(CT):
                    for t in range(KT):
                        cols = slice(P * m, P * (m + 1))
                        mm = split_product(pslot[:, slot_k, CH * m:CH * (m + 1)], (wrh[:, t, cols], wrl[:, t, cols]),
                                           (fxh[:, t, :], fxl[:, t, :]), t == 0, t == KT - 1)
                mm.then_inc(filled, 1)

            pe.wait_ge(prep_act, 3)
            pe.wait_ge(prep_dve, 6)
            for k in range(NCH):
                if k >= PSLOTS:
                    pe.wait_ge(emptied[k % PSLOTS], k // PSLOTS)
                reduce_chunk(k, k % PSLOTS, k + 1)

            def rows_of(image, ct, row, n):
                return image[:, ct].rearrange("p h w -> p (h w)")[:, S * row:S * (row + n)]

            def batch(b, last):
                pl = place_last if last else place

                def begin(u, *sources):
                    n = PRE + pl[u]
                    need = {n % PSLOTS: n // PSLOTS}
                    for v in sources:
                        m = PRE + pl[v]
                        need[m % PSLOTS] = max(need.get(m % PSLOTS, 0), m // PSLOTS + 1)
                    for k in sorted(need):
                        pe.wait_ge(emptied[k], need[k] + (PER // PSLOTS) * b)
                    return n % PSLOTS

                def transposes(u, part, tiles=8, sources=()):
                    k = begin(u, *sources)
                    for n in range(tiles):
                        t = nc.tensor.transpose(pslot[:, k, P * n:P * (n + 1)], part(n), ident[:])
                    t.then_inc(filled, 1)

                def transform(u, source, matrix, more=None):
                    ts = transposed[source] % TSLOTS
                    k = begin(u, source)
                    for n in range(8):
                        dst, m = pslot[:, k, P * n:P * (n + 1)], dft[:, matrix(n), :]
                        if u[0] == "D4":
                            dst = pslot[:, k, CH * (n // 4):CH * (n // 4 + 1)].rearrange(
                                "p (a g w) -> p a g w", a=2, g=4)[:, :, n % 4, :]
                            m = m.rearrange("p (a w) -> p a w", a=2)
                        mm = nc.tensor.matmul(dst, tt[:, ts, P * n:P * (n + 1)], m, start=(n % 4 == 0), stop=True,
                                              skip_group_check=True)
                    if more is not None:
                        mm = more(mm)
                    mm.then_inc(filled, 1)

                for u in (order_last if last else order):
                    kind, i = u
                    ct, q = i // 4, i % 4
                    if kind == "A":
                        reduce_chunk(i, begin(u), i + 1 + NCH * (b + 1))
                    elif kind == "CS":
                        pe.wait_ge(small, small_at("tot", b))
                        for t in range(CT):
                            mm = nc.tensor.matmul(psmall[0:HG, 0:1], g1_sb[:, t, :], tot[:, t:t + 1],
                                                  start=(t == 0), stop=(t == CT - 1))
                        mm.then_inc(gate_mm, 1)
                        pe.wait_ge(small, small_at("rdiag", b))
                        k = begin(u)
                        mm = nc.tensor.matmul(pslot[:, k, 0:CT * P], ones[:], rdiag[:].rearrange("p a b -> p (a b)"),
                                              start=True, stop=True)
                        mm.then_inc(filled, 1)
                    elif kind == "T1":
                        if i == 0:
                            pe.wait_ge(relu_done, NCONV * CT * (b + 1))
                        transposes(u, lambda n: rows_of(xr, ct, 16 * q + 2 * n, 2))
                    elif kind == "R1":
                        pe.wait_ge(e_sum, 2 * (3 * ct + q + 1) + E_PER * b)
                        transposes(u, lambda n: tt[:, transposed[u] % TSLOTS, P * n:P * (n + 1)], 8 if q < 2 else 1)
                    elif kind == "D1":
                        def gram(mm):
                            if q < 3:
                                pe.wait_ge(mirrored, mirrored_at(i) + MIRRORED_PER * b)
                                ta, tb = transposed[("T1", i)] % TSLOTS, transposed[("R1", i)] % TSLOTS
                                rows = slice(0, P if q < 2 else S)
                                for n in range(8 if q < 2 else 1):
                                    mm = nc.tensor.matmul(pgram[:, P * ct:P * (ct + 1)], tt[rows, ta, P * n:P * (n + 1)],
                                                          tt[rows, tb, P * n:P * (n + 1)], start=(i == 0 and n == 0),
                                                          stop=(q == 2), skip_group_check=True)
                            return mm
                        transform(u, ("T1", i), lambda n: D1, gram)
                    elif kind == "T2":
                        transposes(u, lambda n: rows_of(Y, ct, 16 * q + 2 * n, 2), sources=[("D1", 4 * ct + 3)])
                        if i == 1:
                            pe.wait_ge(hid_ready, b + 1)
                            for t in range(CT):
                                mm = nc.tensor.matmul(psmall[:, 1 + t:2 + t], g2_sb[:, P * t:P * (t + 1)], hid[:],
                                                      start=True, stop=True)
                            mm.then_inc(gate_mm, 1)
                    elif kind == "D2":
                        transform(u, ("T2", i), lambda n: D2S if q == 0 and n == 0 else D2)
                    elif kind == "T3":
                        if q == 0:
                            pe.wait_ge(z_re, ct + 1 + CT * b)
                        pe.wait_ge(z_done, i + 1 + 8 * b)
                        transposes(u, lambda n: Z[:, n, 1:3].rearrange("p r k -> p (r k)"))
                    elif kind == "D3":
                        transform(u, ("T3", i), lambda n: D3S if q == 0 and n == 0 else D3)
                    elif kind == "W":
                        pe.wait_ge(small, small_at("attn", b))
                        k = begin(u)
                        for t in range(CT):
                            mm = nc.tensor.matmul(pslot[:, k, 512 * t:512 * t + KT * P], attn[:, t, :],
                                                  pw1[:, t, :], start=True, stop=True)
                        mm.then_inc(filled, 1)
                    elif kind == "T4":
                        transposes(u, lambda n: Y[:, n // 4].rearrange("p k h -> p (k h)")[:, 4 * i + n % 4::32],
                                   sources=[("D3", 7)])
                    elif kind == "D4":
                        transform(u, ("T4", i), lambda n: D4)
                    else:
                        half = int(kind[1])
                        if i == 0 and half == 0:
                            wait_emptied(pe, ("W", 0), b, last)
                            pe.wait_ge(edge_ready, b + 1)
                            for o in range(KT):
                                for t in range(CT):
                                    for w in (wah, wal):
                                        mm = nc.tensor.matmul(psmall[:, 128 + 32 * o:160 + 32 * o],
                                                              w[:, t, P * o:P * (o + 1)].bitcast(F32), edge[:, t, :],
                                                              start=(t == 0 and w is wah), stop=(t == 1 and w is wal))
                            mm.then_inc(edge_mm, 1)
                            pe.wait_ge(e_low, 3 * CT * (b + 1))
                        k = begin(u, ("W", 0))
                        banks = [(pslot[:, k, CH * m:CH * (m + 1)], slice(P * (2 * half + m), P * (2 * half + m + 1)))
                                 for m in range(2)]
                        for dst, cols in banks:
                            for t in range(CT):
                                w = (wah[:, t, cols], wal[:, t, cols])
                                split_product(dst[:, 0:CH // 2], w, [part[:, t, 4 * S * i:4 * S * (i + 1)] for part in (eh, el)],
                                              first=(t == 0), last=False)
                                top = S * (S // 2 - 4 * i) + S
                                v = [part[:, t, top:top - CH // 2:-1] for part in (eh, el)]
                                split_product(dst[:, CH // 2:CH], w, v, first=False, last=False)
                        wait_emptied(pe, ("D4", i), b, last)
                        for dst, cols in banks:
                            for t in range(CT):
                                mm = split_product(dst, (pwh[:, t, cols], pwl[:, t, cols]),
                                                   (fxh[:, CT * (i % 2) + t, :], fxl[:, CT * (i % 2) + t, :]),
                                                   first=False, last=(t == CT - 1))
                        mm.then_inc(filled, 1)

            with pe.Fori(0, B - 1) as b:
                batch(b, False)
            batch(B - 1, True)

        @block.scalar
        def _(act):
            act.wait_ge(consts_in, 16 * 11)
            act.wait_ge(prep_dve, 1)
            nc.scalar.activation(t_b[:], t_a[:], ACT.Sqrt).then_inc(prep_act, 1)
            nc.scalar.activation(wrh[:], wr_raw, ACT.Copy).then_inc(prep_act, 1)
            nc.scalar.activation(pwh[:], pw_raw, ACT.Copy).then_inc(prep_act, 1)
            act.wait_ge(cleared, 4)

            def split_high(k, full_count, count):
                if count:
                    act.wait_ge(filled, count)
                act.wait_ge(xs_full[k % 2], full_count)
                nc.scalar.activation(fxh[:], xs[:, k % 2], ACT.Copy).then_inc(x_high, 1)

            def pad_chunk(k, slot_k):
                for m in range(CT):
                    a = nc.scalar.activation(
                        padded[:, m, 1 + 8 * k:9 + 8 * k, 1:S + 1],
                        pslot[:, slot_k, CH * m:CH * (m + 1)].rearrange("p (h w) -> p h w", w=S),
                        ACT.Identity, bias=cv[:, REDUCE_B, m:m + 1])
                a.then_inc(emptied[slot_k], 1)

            def centre(j):
                for t in range(CT):
                    nc.scalar.activation(conv_out(t, j), conv_view(t, j, 4), ACT.Copy,
                                         scale=dw_sb[:, t, 4:5]).then_inc(centred, 1)

            def relu(j, base):
                act.wait_ge(tapped, CONV_OPS * (j + 1) + base)
                for t in range(CT):
                    nc.scalar.activation(conv_out(t, j), conv_out(t, j), ACT.Relu, scale=bn_s[:, t:t + 1],
                                         bias=bn_b[:, t:t + 1], accum_out=sums[:, t, j:j + 1]).then_inc(relu_done, 1)

            def squares(j, base):
                act.wait_ge(relu_done, CT * (j + 1) + base)
                for t in range(CT):
                    for half in range(2):
                        n = 2 * (CT * j + t) + half
                        if not (isinstance(base, int) and base + n == 0):
                            act.wait_ge(stats, n + 2 * base)
                        r = CONV_ROWS * j + 8 * half
                        nc.scalar.activation(pgram[:].rearrange("p (h w) -> p h w", w=S), xr[:, t, r:r + 8, :],
                                             ACT.Square, accum_out=ssq[:, t, 2 * j + half:2 * j + half + 1]).then_inc(stats, 1)

            for k in range(NCH):
                split_high(k, 16 * (k // 2 + 1), k)
                act.wait_ge(filled, k + 1)
                pad_chunk(k, k % PSLOTS)
                act.wait_ge(emptied[k % PSLOTS], k // PSLOTS + 1)
                if k % 2 == 1:
                    centre(k // 2)
            act.wait_ge(prep_dve, 4)
            for j in range(NCONV):
                relu(j, 0)
                squares(j, 0)

            def batch(b, last):
                wait = lambda u: wait_filled(act, u, b, last)
                done_taps = CONV_OPS * NCONV * (b + 1)
                done_relu = NCONV * CT * (b + 1)

                relu_at = [next(p for p in range(2 * NCH) if conv_before(p) >= CONV_OPS * (j + 1))
                           for j in range(NCONV)]

                def copy_tile(u):
                    k = slot(u, last)
                    nc.scalar.activation(tt[:, transposed[u] % TSLOTS, :], pslot[:, k, :],
                                         ACT.Copy).then_inc(emptied[k], 1)

                def split_next(k):
                    if not last and k < NCH:
                        position_before = position(("A", k - 1), b, last) + 1 if k else None
                        if k:
                            act.wait_ge(filled, position_before)
                        act.wait_ge(xs_full[k % 2], 16 * (k // 2 + 1) + XS_PER * (b + 1))
                        nc.scalar.activation(fxh[:], xs[:, k % 2], ACT.Copy).then_inc(x_high, 1)

                for u in (order_last if last else order):
                    kind, i = u
                    ct, q = i // 4, i % 4
                    if kind in ("CS", "T3", "R1"):
                        if kind == "R1":
                            at, n = (1024 * q, 1024) if q < 2 else (2048, S + 2)
                            blk = 3 * ct + q
                            act.wait_ge(e_sum, 2 * (blk + 1) + E_PER * b)
                            nc.scalar.activation(eh[:, ct, at:at + n], tt[:, transposed[u] % TSLOTS, 0:n],
                                                 ACT.Copy).then_inc(e_high, 1)
                            if i == 1:
                                split_next(0)
                        if kind == "CS":
                            act.wait_ge(small, small_at("tsq", b))
                            nc.scalar.activation(nrm[:], tsq[:], ACT.Sqrt).then_inc(nrm_ready, 1)
                            act.wait_ge(gate_mm, 1 + 2 * b)
                            nc.scalar.activation(hid[:], psmall[0:HG, 0:1], ACT.Relu, bias=gb1[:],
                                                 scale=1.0 / (S * S)).then_inc(hid_ready, 1)
                        continue
                    if kind in ("P0", "P1"):
                        p = 2 * i + int(kind[1])
                        if p == 0:
                            act.wait_ge(edge_mm, b + 1)
                            nc.scalar.activation(z0[:].rearrange("p a b -> p (a b)"), psmall[:, 128:256],
                                                 ACT.Copy).then_inc(edge_out, 1)
                            if not last:
                                wait_emptied(act, ("A", 7), b)
                                centre(3)
                        for j in range(NCONV):
                            if not last and p == relu_at[j]:
                                relu(j, done_taps)
                                squares(j, done_relu)
                        continue
                    wait(u)
                    k = slot(u, last)
                    if kind in ("T1", "T2", "T4"):
                        copy_tile(u)
                    elif kind == "A":
                        pad_chunk(i, k)
                        split_next(i + 1)
                        if i in (3, 4, 6):
                            wait_emptied(act, ("A", i), b)
                            if i == 3:
                                wait_emptied(act, ("A", 2), b)
                                centre(0)
                            elif i == 4:
                                centre(1)
                            else:
                                wait_emptied(act, ("A", 5), b)
                                wait_emptied(act, ("A", 4), b)
                                centre(2)
                    elif kind == "D1":
                        dst = Y[:, ct, :, 16 * q:16 * q + 16].rearrange("p k (n a) -> p k n a", a=2)
                        src = pslot[:, k, :].rearrange("p (n k a) -> p k n a", n=8, a=2)
                        nc.scalar.activation(dst, src, ACT.Copy).then_inc(emptied[k], 1)
                    elif kind == "D2":
                        v = pslot[:, k, :].rearrange("p (n r k) -> p n r k", n=8, r=2)
                        if i >= 1:
                            wait(("T3", i - 1))
                        nc.scalar.activation(Z[:, :, 0:2, :], v, ACT.Copy).then_inc(emptied[k], 1)
                        wait_emptied(act, u, b, last)
                        if q == 0:
                            nc.scalar.activation(packed[:], Z[:, 0, 0:2, 0:S:32], ACT.Square).then_inc(packed_sq, 1)
                            act.wait_ge(packed_sq, ct + 1 + CT * b)
                        act.wait_ge(z_im, i + 1 + 8 * b)
                        nc.scalar.activation(Z[:, :, 0:2, :], Z[:, :, 0:2, :], ACT.Square).then_inc(sq_ready, 1)
                        if i == 1:
                            act.wait_ge(gate_mm, 2 + 2 * b)
                            for t in range(CT):
                                a = nc.scalar.activation(gexp[:, t:t + 1], psmall[:, 1 + t:2 + t], ACT.Exp,
                                                         scale=-1.0, bias=ng_b2[:, t:t + 1])
                            a.then_inc(gexp_ready, 1)
                        if i == 3:
                            act.wait_ge(small, small_at("nmax", b))
                            for t in range(CT):
                                a = nc.scalar.activation(expd[:, t, :], scores[:, t, :], ACT.Exp,
                                                         bias=nmax[:, t:t + 1], accum_out=esum[:, t:t + 1])
                                a.then_inc(exp_ready, 1)
                    elif kind == "D3":
                        dst = Y[:, ct, 16 * q:16 * q + 16, :].rearrange("p k h -> p (k h)")
                        nc.scalar.activation(dst, pslot[:, k, :], ACT.Copy).then_inc(emptied[k], 1)
                    elif kind == "W":
                        nc.scalar.activation(wah[:].rearrange("p a b -> p (a b)"), pslot[:, k, :], ACT.Copy,
                                             scale=0.5).then_inc(w_high, 1)
                    elif kind == "D4":
                        if i == 0:
                            act.wait_ge(small, small_at("gate", b))
                        for t in range(CT):
                            a = nc.scalar.activation(
                                fxh[:, CT * (i % 2) + t, :], pslot[:, k, CH * t:CH * (t + 1)],
                                ACT.Copy, scale=gate[:, t:t + 1])
                        a.then_inc(f_high, 1)

            with act.Fori(0, B - 1) as b:
                batch(b, False)
            batch(B - 1, True)

        @block.vector
        def _(dve):
            dve.wait_ge(consts_in, 16 * 11)
            nc.vector.tensor_scalar(t_a[:], cv[:, BN_VAR, :], BN_EPS, None, ALU.add).then_inc(prep_dve, 1)
            nc.vector.tensor_scalar(ng_b2[:], cv[:, GATE_B2, :], -1.0, None, ALU.mult)
            dve.wait_ge(prep_act, 1)
            nc.vector.reciprocal(rn[:], t_b[:]).then_inc(prep_dve, 1)
            dve.wait_ge(prep_dve, 2)
            nc.vector.tensor_tensor(bn_s[:], cv[:, BN_G, :], rn[:], ALU.mult).then_inc(prep_dve, 1)
            nc.vector.tensor_tensor(nrm[:], cv[:, DW_B, :], cv[:, BN_MEAN, :], ALU.subtract)
            dve.drain()
            nc.vector.tensor_tensor(rnt[:], nrm[:], bn_s[:], ALU.mult)
            dve.drain()
            nc.vector.tensor_tensor(bn_b[:], rnt[:], cv[:, BN_BETA, :], ALU.add).then_inc(prep_dve, 1)
            dve.wait_ge(prep_act, 3)
            nc.vector.tensor_tensor(wrl[:], wr_raw, wrh[:].bitcast(F32), ALU.subtract).then_inc(prep_dve, 1)
            nc.vector.tensor_tensor(pwl[:], pw_raw, pwh[:].bitcast(F32), ALU.subtract).then_inc(prep_dve, 1)

            def split_low(k, count):
                dve.wait_ge(x_high, count)
                nc.vector.tensor_tensor(fxl[:], xs[:, k % 2], fxh[:].bitcast(F32), ALU.subtract).then_inc(x_low, 1)

            def conv_step(n, base, centre_base, chunks=None):
                j, tap, t = n // CONV_OPS, TAPS[n % CONV_OPS // CT], n % CT
                if n % CONV_OPS == 0:
                    dve.wait_ge(centred, CT * (j + 1) + centre_base)
                    if chunks is not None:
                        c = min(2 * j + 2, NCH - 1)
                        dve.wait_ge(emptied[c % PSLOTS], c // PSLOTS + 1)
                if n >= CT:
                    dve.wait_ge(tapped, n - CT + 1 + base)
                nc.vector.scalar_tensor_tensor(out=conv_out(t, j), in0=conv_view(t, j, tap),
                                               scalar=dw_sb[:, t, tap:tap + 1], in1=conv_out(t, j),
                                               op0=ALU.mult, op1=ALU.add).then_inc(tapped, 1)

            for k in range(NCH):
                if k:
                    dve.wait_ge(filled, k)
                split_low(k, k + 1)
            for n in range(CONV_OPS * NCONV):
                conv_step(n, 0, 0, chunks=True)

            def batch(b, last):
                wait = lambda u: wait_filled(dve, u, b, last)
                count = [0]
                early = [0]
                conv_base = CONV_OPS * NCONV * (b + 1)
                centre_base = CT * NCONV * (b + 1)

                def step(ins, name=None, wait_for=True):
                    count[0] += 1
                    ins.then_inc(small, 1)
                    if name is not None:
                        assert SMALL_STEPS[name] == count[0], (name, count[0])
                    if wait_for:
                        dve.wait_ge(small, count[0] + SMALL_PER * b)

                def e_block(blk, b):
                    u = ("R1", blk // 3 * 4 + blk % 3)
                    before = made.index(u) - TSLOTS
                    if before >= 0:
                        v = made[before]
                        wait((used_by[v[0]], v[1]))
                    t, r = blk // 3, 16 * (blk % 3)
                    n = 16 if r < 32 else 2
                    dst = tt[:, transposed[u] % TSLOTS, 0:S * n].rearrange("p (h w) -> p h w", w=S)
                    top = S - r
                    nc.vector.tensor_tensor(dst[:, :, 1:S], xr[:, t, r:r + n, 1:S],
                                            xr[:, t, top:top - n:-1, S - 1:0:-1], ALU.add).then_inc(e_sum, 1)
                    nc.vector.tensor_tensor(dst[:, :, 0], xr[:, t, r:r + n, 0],
                                            xr[:, t, top:top - n:-1, 0], ALU.add).then_inc(e_sum, 1)

                def conv_early(n):
                    if last:
                        return
                    for _ in range(n):
                        if early[0] < CONV_EARLY:
                            conv_step(early[0], conv_base, centre_base)
                            early[0] += 1

                for u in (order_last if last else order):
                    kind, i = u
                    ct, q = i // 4, i % 4
                    k = slot(u, last)
                    if kind == "A":
                        if i + 1 < NCH:
                            wait(u)
                            split_low(i + 1, i + 2 + NCH * (b + 1))
                    elif kind == "CS":
                        dve.wait_ge(stats, 2 * NCONV * CT * (b + 1))
                        step(nc.vector.tensor_reduce(tot[:], sums[:], AX_X, ALU.add), "tot")
                        step(nc.vector.tensor_reduce(tsq[:], ssq[:], AX_X, ALU.add), "tsq")
                        dve.wait_ge(nrm_ready, b + 1)
                        step(nc.vector.tensor_scalar(nrm[:], nrm[:], NORM_EPS, None, ALU.max))
                        step(nc.vector.reciprocal(rn[:], nrm[:]), "rn")
                        step(nc.vector.tensor_tensor(rnt[:], rn[:], cv[:, TEMP, :], ALU.mult), "rnt")
                        for t in range(CT):
                            step(nc.vector.tensor_scalar(rdiag[:, t, :], ident[:], rn[:, t:t + 1], None, ALU.mult))
                        nc.vector.tensor_copy(xr[:, :, S, :], xr[:, :, 0, :]).then_inc(wrapped, 1)
                        dve.wait_ge(wrapped, b + 1)
                        e_block(0, b)
                        wait(u)
                        nc.vector.tensor_copy(cscale[:].rearrange("p a b -> p (a b)"),
                                              pslot[:, k, 0:CT * P]).then_inc(emptied[k], 1)
                    elif kind == "R1":
                        blk = 3 * ct + q
                        at, n = (1024 * q, 1024) if q < 2 else (2048, S + 2)
                        ta, tb = transposed[("T1", i)] % TSLOTS, transposed[u] % TSLOTS
                        dve.wait_ge(e_high, blk + 1 + 3 * CT * b)
                        nc.vector.tensor_tensor(el[:, ct, at:at + n], tt[:, tb, 0:n],
                                                eh[:, ct, at:at + n].bitcast(F32), ALU.subtract).then_inc(e_low, 1)
                        dve.wait_ge(e_low, blk + 1 + 3 * CT * b)
                        wait(u)
                        wait_emptied(dve, ("T1", i), b, last)
                        rows, cols = (slice(0, P), slice(0, 1024)) if q < 2 else (slice(0, S), slice(0, P))
                        nc.vector.tensor_tensor(tt[rows, tb, cols], pslot[rows, k, cols], tt[rows, ta, cols],
                                                ALU.subtract).then_inc(mirrored, 1)
                        base = MIRRORED_PER // CT * ct + (0, 2, 3)[q]
                        dve.wait_ge(mirrored, base + 1 + MIRRORED_PER * b)
                        dve.sem_inc(emptied[k], 1)
                        if q != 1:
                            nc.vector.tensor_scalar(tt[0:S, tb, 0:P], tt[0:S, tb, 0:P], 0.5, None,
                                                    ALU.mult).then_inc(mirrored, 1)
                        if blk + 1 < 3 * CT:
                            e_block(blk + 1, b)
                        if i == 1 and not last:
                            split_low(0, 1 + NCH * (b + 1))
                        if i == 6:
                            dve.wait_ge(e_low, 3 * CT * (b + 1))
                            step(nc.vector.tensor_tensor(edge[:], eh[:, :, 32 * S:0:-S].bitcast(F32),
                                                         el[:, :, 32 * S:0:-S].bitcast(F32), ALU.add), "edge0")
                            step(nc.vector.tensor_tensor(edge[:], edge[:], eh[:, :, 33 * S:S:-S].bitcast(F32),
                                                         ALU.subtract), "edge1")
                            nc.vector.tensor_tensor(edge[:], edge[:], el[:, :, 33 * S:S:-S].bitcast(F32),
                                                    ALU.subtract).then_inc(edge_ready, 1)
                    elif kind == "D2":
                        wait_emptied(dve, u, b, last)
                        nc.vector.scalar_tensor_tensor(out=Z[:, :, 2, :], in0=Z[:, :, 0, :], scalar=2.0, in1=Z[:, :, 1, :],
                                                       op0=ALU.mult, op1=ALU.mult).then_inc(z_im, 1)
                        conv_early(1 if i >= 1 else 0)
                        dve.wait_ge(sq_ready, i + 1 + 8 * b)
                        nc.vector.tensor_tensor(Z[:, :, 1, :], Z[:, :, 0, :], Z[:, :, 1, :],
                                                ALU.subtract).then_inc(z_done, 1)
                        if q == 0:
                            dve.wait_ge(z_done, i + 1 + 8 * b)
                            nc.vector.tensor_copy(Z[:, 0, 1:3, 0:S:32], packed[:]).then_inc(z_re, 1)
                        if i == 2:
                            dve.wait_ge(gexp_ready, b + 1)
                            step(nc.vector.tensor_scalar(gplus[:], gexp[:], 1.0, None, ALU.add), "gplus")
                            step(nc.vector.reciprocal(gate[:], gplus[:]), "gate")
                            wait(("D1", 6))
                            wait_emptied(dve, ("CS", 0), b, last)
                            for t in range(CT):
                                for g in range(4):
                                    rows = slice(32 * g, 32 * g + 32)
                                    step(nc.vector.tensor_copy(gram_b[rows, t, :],
                                                               pgram[rows, P * t + 32 * g:P * t + 32 * g + 32]),
                                         wait_for=(t == CT - 1 and g == 3))
                            for t in range(CT):
                                step(nc.vector.transpose(gram_t[:, t, :], gram_b[:, t, :]), wait_for=(t == CT - 1))
                            step(nc.vector.tensor_tensor(gram_b[:], gram_b[:], gram_t[:], ALU.add))
                            for t in range(CT):
                                for g in range(4):
                                    rows = slice(32 * g, 32 * g + 32)
                                    step(nc.vector.scalar_tensor_tensor(
                                        out=scores[rows, t, :], in0=gram_b[rows, t, :],
                                        scalar=rnt[rows, t:t + 1], in1=cscale[rows, t, 32 * g:32 * g + 32],
                                        op0=ALU.mult, op1=ALU.mult), wait_for=(t == CT - 1 and g == 3))
                            step(nc.vector.tensor_reduce(nmax[:], scores[:], AX_X, ALU.max, negate=True), "nmax")
                        if i == 4:
                            dve.wait_ge(exp_ready, 2 * (b + 1))
                            step(nc.vector.reciprocal(rsum[:], esum[:]), "rsum")
                            for t in range(CT):
                                for g in range(4):
                                    rows = slice(32 * g, 32 * g + 32)
                                    step(nc.vector.tensor_scalar(attn[rows, t, 32 * g:32 * g + 32], expd[rows, t, :],
                                                                 rsum[rows, t:t + 1], None, ALU.mult), wait_for=False)
                    elif kind == "T3":
                        wait(u)
                        nc.vector.tensor_copy(tt[:, transposed[u] % TSLOTS, :], pslot[:, k, :]).then_inc(emptied[k], 1)
                        conv_early(2 if i == 7 else 1)
                    elif kind == "W":
                        dve.wait_ge(w_high, b + 1)
                        nc.vector.scalar_tensor_tensor(
                            out=wal[:].rearrange("p a b -> p (a b)"), in0=pslot[:, k, :], scalar=0.5,
                            in1=wah[:].rearrange("p a b -> p (a b)").bitcast(F32),
                            op0=ALU.mult, op1=ALU.subtract).then_inc(emptied[k], 1)
                    elif kind == "D4":
                        dve.wait_ge(f_high, i + 1 + NCH * b)
                        for t in range(CT):
                            low = nc.vector.scalar_tensor_tensor(
                                out=fxl[:, CT * (i % 2) + t, :], in0=pslot[:, k, CH * t:CH * (t + 1)],
                                scalar=gate[:, t:t + 1],
                                in1=fxh[:, CT * (i % 2) + t, :].bitcast(F32),
                                op0=ALU.mult, op1=ALU.subtract)
                        low.then_inc(emptied[k], 1)
                    elif kind in ("P0", "P1"):
                        half = int(kind[1])
                        dve.wait_ge(res_full[half][i % 2], 32 * (i // 2 + 1) + RES_PER * b)
                        if i == 0 and half == 0:
                            dve.wait_ge(edge_out, b + 1)
                        tiles = slice(2 * half, 2 * half + 2)
                        low = xs[:, i % 2, tiles, CH // 2:CH:S]
                        nc.vector.tensor_tensor(low, low, z0[:, tiles, 4 * i:4 * i + 4], ALU.add).then_inc(edge_added, 1)
                        dve.wait_ge(edge_added, 2 * i + half + 1 + 2 * NCH * b)
                        wait(u)
                        for m in range(2):
                            o = 2 * half + m
                            add = nc.vector.scalar_tensor_tensor(
                                out=xs[:, i % 2, o, :], in0=pslot[:, k, CH * m:CH * (m + 1)],
                                scalar=po_b[:, o:o + 1], in1=xs[:, i % 2, o, :],
                                op0=ALU.add, op1=ALU.add)
                        add.then_inc(emptied[k], 1)
                        if not last:
                            p = 2 * i + half
                            for n in range(conv_before(p), conv_before(p + 1)):
                                conv_step(n, conv_base, centre_base)
                assert count[0] == SMALL_PER, count
                assert last or early[0] == CONV_EARLY

            with dve.Fori(0, B - 1) as b:
                batch(b, False)
            batch(B - 1, True)


_VECTORS = ["reduce_b", "dw_b", "bn_gamma", "bn_beta", "bn_mean", "bn_var", "gate_b2"]


def kernel(**inputs):
    import concourse.bacc as _bacc
    from concourse.bass_utils import run_bass_kernel_spmd as _run

    a = {k.replace("L0_conv_", ""): np.asarray(v) for k, v in inputs.items()}
    mid, cin = a["reduce_w"].shape

    def tiles(v):
        return v.reshape(-1, P).T

    def weight(w):
        return w.T.reshape(-1, P, w.shape[0]).transpose(1, 0, 2)

    temp = np.repeat(a["temperature"].reshape(-1), mid // a["temperature"].size)
    layout = {
        "x": a["x"],
        "reduce_wt": weight(a["reduce_w"]),
        "dw": a["dw_w"].reshape(-1, P, 9).transpose(1, 0, 2),
        "channel": np.stack([tiles(a[n]) for n in _VECTORS] + [tiles(temp)], axis=1),
        "bias_out": tiles(a["post_b"]),
        "gate_w1t": weight(a["gate_w1"]),
        "gate_b1": a["gate_b1"].reshape(-1, 1),
        "gate_w2t": a["gate_w2"].T,
        "post_wt": weight(a["post_w"]),
        "fourier": fourier_matrices(),
        "identity": np.eye(P, dtype=np.float32),
    }
    nc = _bacc.Bacc("TRN2", target_bir_lowering=False, num_devices=1, dynamic_dma_scratch_size=256)
    arrays, args = {}, {}
    for name, v in layout.items():
        v = np.ascontiguousarray(v)
        arrays[f"in_{name}"] = v
        args[name] = nc.dram_tensor(f"in_{name}", v.shape, mybir.dt.from_np(v.dtype), kind="ExternalInput").ap()
    out = nc.dram_tensor("out_y", a["x"].shape, F32, kind="ExternalOutput").ap()
    build(nc, out=out, **args)
    r = _run(nc, [arrays], core_ids=[0])
    return r.results[0]["out_y"]
```
